# Optimizing a Trainium2 kernel written in Bass

```python
import numpy as np
import jax
import jax.numpy as jnp

def _softmax(x, axis=-1):
    return jax.nn.softmax(x, axis=axis)

def _gelu(x):
    return jax.nn.gelu(x, approximate=True)

def _silu(x):
    return jax.nn.silu(x)

def _sigmoid(x):
    return jax.nn.sigmoid(x)

def _layernorm(x, axis=-1, eps=1e-05):
    m = jnp.mean(x, axis=axis, keepdims=True)
    v = jnp.var(x, axis=axis, keepdims=True)
    return (x - m) / jnp.sqrt(v + eps)

def _scatter_add(tgt, idx, src, axis=0):
    return tgt.at[idx].add(src)

def _segment_sum(src, seg, n):
    return jax.ops.segment_sum(src, seg, n)
kernel_name = 'mk_dlrm_tower_d1_rec_r8_3ec779'

def setup_inputs(seed: int=0):
    np.random.seed(seed)
    _w = jnp.asarray

    def _rec_inputs():
        import jax
        import jax.numpy as jnp
        _tk = jax.random.key(seed)
        dense_ctx = jax.random.normal(jax.random.fold_in(_tk, 190), (512, 16), jnp.float32)
        ids = jnp.stack([jax.random.randint(jax.random.fold_in(_tk, 200 + f), (512,), 0, v, jnp.int32) for f, v in enumerate([12500, 1250, 12500, 1000, 125000, 1250, 1000, 1000, 1000, 1000, 1250, 12500, 12500, 12500, 1250, 12500, 12500, 1250, 1000, 1000, 1250, 1250, 12500, 1250, 1250, 1000, 1000, 1250, 1250, 1000, 1000, 1250])], axis=1)
        tbl_0 = 0.05 * jax.random.normal(jax.random.fold_in(_tk, 500 + 0), (12500, 128), jnp.float32)
        tbl_1 = 0.05 * jax.random.normal(jax.random.fold_in(_tk, 500 + 1), (1250, 128), jnp.float32)
        tbl_2 = 0.05 * jax.random.normal(jax.random.fold_in(_tk, 500 + 2), (12500, 128), jnp.float32)
        tbl_3 = 0.05 * jax.random.normal(jax.random.fold_in(_tk, 500 + 3), (1000, 128), jnp.float32)
        tbl_4 = 0.05 * jax.random.normal(jax.random.fold_in(_tk, 500 + 4), (125000, 128), jnp.float32)
        tbl_5 = 0.05 * jax.random.normal(jax.random.fold_in(_tk, 500 + 5), (1250, 128), jnp.float32)
        tbl_6 = 0.05 * jax.random.normal(jax.random.fold_in(_tk, 500 + 6), (1000, 128), jnp.float32)
        tbl_7 = 0.05 * jax.random.normal(jax.random.fold_in(_tk, 500 + 7), (1000, 128), jnp.float32)
        tbl_8 = 0.05 * jax.random.normal(jax.random.fold_in(_tk, 500 + 8), (1000, 128), jnp.float32)
        tbl_9 = 0.05 * jax.random.normal(jax.random.fold_in(_tk, 500 + 9), (1000, 128), jnp.float32)
        tbl_10 = 0.05 * jax.random.normal(jax.random.fold_in(_tk, 500 + 10), (1250, 128), jnp.float32)
        tbl_11 = 0.05 * jax.random.normal(jax.random.fold_in(_tk, 500 + 11), (12500, 128), jnp.float32)
        tbl_12 = 0.05 * jax.random.normal(jax.random.fold_in(_tk, 500 + 12), (12500, 128), jnp.float32)
        tbl_13 = 0.05 * jax.random.normal(jax.random.fold_in(_tk, 500 + 13), (12500, 128), jnp.float32)
        tbl_14 = 0.05 * jax.random.normal(jax.random.fold_in(_tk, 500 + 14), (1250, 128), jnp.float32)
        tbl_15 = 0.05 * jax.random.normal(jax.random.fold_in(_tk, 500 + 15), (12500, 128), jnp.float32)
        tbl_16 = 0.05 * jax.random.normal(jax.random.fold_in(_tk, 500 + 16), (12500, 128), jnp.float32)
        tbl_17 = 0.05 * jax.random.normal(jax.random.fold_in(_tk, 500 + 17), (1250, 128), jnp.float32)
        tbl_18 = 0.05 * jax.random.normal(jax.random.fold_in(_tk, 500 + 18), (1000, 128), jnp.float32)
        tbl_19 = 0.05 * jax.random.normal(jax.random.fold_in(_tk, 500 + 19), (1000, 128), jnp.float32)
        tbl_20 = 0.05 * jax.random.normal(jax.random.fold_in(_tk, 500 + 20), (1250, 128), jnp.float32)
        tbl_21 = 0.05 * jax.random.normal(jax.random.fold_in(_tk, 500 + 21), (1250, 128), jnp.float32)
        tbl_22 = 0.05 * jax.random.normal(jax.random.fold_in(_tk, 500 + 22), (12500, 128), jnp.float32)
        tbl_23 = 0.05 * jax.random.normal(jax.random.fold_in(_tk, 500 + 23), (1250, 128), jnp.float32)
        tbl_24 = 0.05 * jax.random.normal(jax.random.fold_in(_tk, 500 + 24), (1250, 128), jnp.float32)
        tbl_25 = 0.05 * jax.random.normal(jax.random.fold_in(_tk, 500 + 25), (1000, 128), jnp.float32)
        tbl_26 = 0.05 * jax.random.normal(jax.random.fold_in(_tk, 500 + 26), (1000, 128), jnp.float32)
        tbl_27 = 0.05 * jax.random.normal(jax.random.fold_in(_tk, 500 + 27), (1250, 128), jnp.float32)
        tbl_28 = 0.05 * jax.random.normal(jax.random.fold_in(_tk, 500 + 28), (1250, 128), jnp.float32)
        tbl_29 = 0.05 * jax.random.normal(jax.random.fold_in(_tk, 500 + 29), (1000, 128), jnp.float32)
        tbl_30 = 0.05 * jax.random.normal(jax.random.fold_in(_tk, 500 + 30), (1000, 128), jnp.float32)
        tbl_31 = 0.05 * jax.random.normal(jax.random.fold_in(_tk, 500 + 31), (1250, 128), jnp.float32)
        _rk = jax.random.fold_in(_tk, 7)
        W_top1 = 0.0441942 * jax.random.normal(jax.random.fold_in(_tk, 801), (512, 512), jnp.float32)
        W_top2 = 0.0441942 * jax.random.normal(jax.random.fold_in(_tk, 802), (512, 256), jnp.float32)
        W_top3 = 0.0625 * jax.random.normal(jax.random.fold_in(_tk, 803), (256, 1), jnp.float32)
        b_top1 = jnp.zeros((512,), jnp.float32)
        b_top2 = jnp.zeros((256,), jnp.float32)
        return (dense_ctx, ids, tbl_0, tbl_1, tbl_2, tbl_3, tbl_4, tbl_5, tbl_6, tbl_7, tbl_8, tbl_9, tbl_10, tbl_11, tbl_12, tbl_13, tbl_14, tbl_15, tbl_16, tbl_17, tbl_18, tbl_19, tbl_20, tbl_21, tbl_22, tbl_23, tbl_24, tbl_25, tbl_26, tbl_27, tbl_28, tbl_29, tbl_30, tbl_31, W_top1, b_top1, W_top2, b_top2, W_top3)
    dense_ctx, ids, tbl_0, tbl_1, tbl_2, tbl_3, tbl_4, tbl_5, tbl_6, tbl_7, tbl_8, tbl_9, tbl_10, tbl_11, tbl_12, tbl_13, tbl_14, tbl_15, tbl_16, tbl_17, tbl_18, tbl_19, tbl_20, tbl_21, tbl_22, tbl_23, tbl_24, tbl_25, tbl_26, tbl_27, tbl_28, tbl_29, tbl_30, tbl_31, W_top1, b_top1, W_top2, b_top2, W_top3 = _rec_inputs()

    def _L0_rec_setup():
        import jax, jax.numpy as jnp
        import numpy as np
        B, F, D = (2048, 32, 128)
        key = jax.random.key(seed)
        inputs = jax.random.normal(key, (B, F, D), dtype=jnp.float32)
        return {'inputs': inputs}
    _L0_rec_all = _L0_rec_setup()
    _L0_rec_in = {k: v for k, v in _L0_rec_all.items() if k in ()}
    del _L0_rec_all
    return {'dense_ctx': dense_ctx, 'ids': ids, 'tbl_0': tbl_0, 'tbl_1': tbl_1, 'tbl_2': tbl_2, 'tbl_3': tbl_3, 'tbl_4': tbl_4, 'tbl_5': tbl_5, 'tbl_6': tbl_6, 'tbl_7': tbl_7, 'tbl_8': tbl_8, 'tbl_9': tbl_9, 'tbl_10': tbl_10, 'tbl_11': tbl_11, 'tbl_12': tbl_12, 'tbl_13': tbl_13, 'tbl_14': tbl_14, 'tbl_15': tbl_15, 'tbl_16': tbl_16, 'tbl_17': tbl_17, 'tbl_18': tbl_18, 'tbl_19': tbl_19, 'tbl_20': tbl_20, 'tbl_21': tbl_21, 'tbl_22': tbl_22, 'tbl_23': tbl_23, 'tbl_24': tbl_24, 'tbl_25': tbl_25, 'tbl_26': tbl_26, 'tbl_27': tbl_27, 'tbl_28': tbl_28, 'tbl_29': tbl_29, 'tbl_30': tbl_30, 'tbl_31': tbl_31, 'W_top1': W_top1, 'b_top1': b_top1, 'W_top2': W_top2, 'b_top2': b_top2, 'W_top3': W_top3}

def reference(dense_ctx, ids, tbl_0, tbl_1, tbl_2, tbl_3, tbl_4, tbl_5, tbl_6, tbl_7, tbl_8, tbl_9, tbl_10, tbl_11, tbl_12, tbl_13, tbl_14, tbl_15, tbl_16, tbl_17, tbl_18, tbl_19, tbl_20, tbl_21, tbl_22, tbl_23, tbl_24, tbl_25, tbl_26, tbl_27, tbl_28, tbl_29, tbl_30, tbl_31, W_top1, b_top1, W_top2, b_top2, W_top3):
    import jax
    import jax.numpy as jnp

    def _L0_rec_ref(inputs):
        import jax, jax.numpy as jnp
        import numpy as np
        B, F, D = (2048, 32, 128)
        dot_products = jnp.einsum('bfd,bgd->bfg', inputs, inputs)
        num_feas = inputs.shape[1]
        iu, ju = jnp.triu_indices(num_feas, k=1)
        return dot_products[:, iu, ju]
    e = jnp.stack([tbl_0[ids[:, 0]], tbl_1[ids[:, 1]], tbl_2[ids[:, 2]], tbl_3[ids[:, 3]], tbl_4[ids[:, 4]], tbl_5[ids[:, 5]], tbl_6[ids[:, 6]], tbl_7[ids[:, 7]], tbl_8[ids[:, 8]], tbl_9[ids[:, 9]], tbl_10[ids[:, 10]], tbl_11[ids[:, 11]], tbl_12[ids[:, 12]], tbl_13[ids[:, 13]], tbl_14[ids[:, 14]], tbl_15[ids[:, 15]], tbl_16[ids[:, 16]], tbl_17[ids[:, 17]], tbl_18[ids[:, 18]], tbl_19[ids[:, 19]], tbl_20[ids[:, 20]], tbl_21[ids[:, 21]], tbl_22[ids[:, 22]], tbl_23[ids[:, 23]], tbl_24[ids[:, 24]], tbl_25[ids[:, 25]], tbl_26[ids[:, 26]], tbl_27[ids[:, 27]], tbl_28[ids[:, 28]], tbl_29[ids[:, 29]], tbl_30[ids[:, 30]], tbl_31[ids[:, 31]]], axis=1)
    z = _L0_rec_ref(e)
    z = z.reshape(z.shape[0], -1)
    h = jnp.concatenate([z, dense_ctx], axis=1)
    h = jnp.maximum(h @ W_top1 + b_top1, 0.0)
    h = jnp.maximum(h @ W_top2 + b_top2, 0.0)
    y = h @ W_top3
    return y

_drawn_inputs = setup_inputs


def setup_inputs(seed=0):
    import zlib

    import numpy as np

    out = dict(_drawn_inputs(seed))
    spreads = {'b_top1': (0.0, 0.1), 'b_top2': (0.0, 0.1)}
    factors = {}
    for name, (base, spread) in spreads.items():
        noise = np.random.default_rng([zlib.crc32(name.encode()), seed]).standard_normal(out[name].shape)
        drawn = base * np.exp(spread * noise) if base else spread * noise
        out[name] = jnp.asarray(drawn.astype(out[name].dtype))
    for name, factor in factors.items():
        out[name] = (out[name] * factor).astype(out[name].dtype)
    return out
```

```python
import concourse.bass as bass
from concourse import mybir
from contextlib import ExitStack

BATCH = 512
TABLES = 32
DIM = 128
DENSE = 16
P = 128
TILES = BATCH // P
QUADRANTS = 4
CHUNKS = TABLES // QUADRANTS
HID1, HID2 = 512, 256
H1B, H2B = HID1 // P, HID2 // P
TGROUP = 4
TGROUPS = TABLES // TGROUP
QUADS = P // QUADRANTS
GQ = 8
GROUNDS = QUADS // GQ


def dlrm_tower(nc, dense, ids, tables, w1, b1, w2, b2, w3, y):
    fp32 = mybir.dt.float32
    i32 = mybir.dt.int32
    ACT = mybir.ActivationFunctionType
    ALU = mybir.AluOpType

    ctx = ExitStack()
    with ctx:
        def sb(name, shape, dt=fp32):
            return ctx.enter_context(nc.sbuf_tensor(name, shape, dt))

        def pb(name, shape):
            return ctx.enter_context(nc.psum_tensor(name, shape, fp32))

        def sem(name):
            return ctx.enter_context(nc.semaphore(name))

        idx = sb("idx", [P, TILES, TABLES], i32)
        emb = sb("emb", [P, TILES, TABLES, DIM])
        embT = sb("embT", [P, 2, P, TABLES])
        ident = sb("ident", [P, P])
        den = sb("den", [P, TILES, DENSE])
        w1s = sb("w1s", [P, CHUNKS, HID1])
        w2s = sb("w2s", [P, H1B, HID2])
        w3s = sb("w3s", [P, H2B])
        b1s = sb("b1s", [P, H1B])
        b2s = sb("b2s", [P, H2B])
        zT = sb("zT", [P, 2, CHUNKS, P])
        h1 = sb("h1", [P, 2, H1B, P])
        h2 = sb("h2", [P, 2, H2B, P])
        ys = sb("ys", [1, BATCH])

        tp = [pb(f"tp{i}", [P, TGROUP, P]) for i in range(2)]
        gram = [pb(f"gram{i}", [P, GQ, P]) for i in range(2)]
        ps1 = pb("ps1", [P, H1B, P])
        ps2 = pb("ps2", [P, 4, P])

        idx_in = sem("idx_in")
        gathered = [[sem(f"gathered_{t}_{g}") for g in range(TGROUPS)] for t in range(TILES)]
        ident_zero = sem("ident_zero")
        ident_ready = sem("ident_ready")
        w1_zero = sem("w1_zero")
        w1_in = sem("w1_in")
        w_in = sem("w_in")
        den_in = sem("den_in")
        z_zero = sem("z_zero")
        tp_full = sem("tp_full")
        tp_even_out = sem("tp_even_out")
        tp_odd_out = sem("tp_odd_out")
        denT_full = sem("denT_full")
        denT_out = sem("denT_out")
        gram_full = sem("gram_full")
        gram_dve_out = sem("gram_dve_out")
        gram_act_out = sem("gram_act_out")
        l1_full = sem("l1_full")
        l1_out = sem("l1_out")
        l2_full = sem("l2_full")
        l2_out = sem("l2_out")
        l3_full = sem("l3_full")
        l3_out = sem("l3_out")
        y_out = sem("y_out")
        block = ctx.enter_context(nc.Block())

        @block.sync
        def _(sp):
            sp.dma_start(idx[:, :, :], ids.rearrange("(t p) f -> p t f", p=P)).then_inc(idx_in, 16)
            sp.dma_start(den[:, :, :], dense.rearrange("(t p) f -> p t f", p=P)).then_inc(den_in, 16)
            sp.wait_ge(w1_zero, 1)
            row = 0
            for f in range(TABLES - 1):
                j, c = f // CHUNKS, f % CHUNKS
                n = TABLES - 1 - f
                sp.dma_start(w1s[32 * j + f + 1:32 * j + TABLES, c, :], w1[row:row + n, :]).then_inc(w1_in, 16)
                row += n
            sp.dma_start(w1s[96:96 + DENSE, CHUNKS - 1, :], w1[row:row + DENSE, :]).then_inc(w1_in, 16)
            sp.dma_start(w2s[:, :, :], w2.rearrange("(k p) n -> p k n", p=P)).then_inc(w_in, 16)
            with nc.allow_non_contiguous_dma(reason="short vectors"):
                sp.dma_start(w3s[:, :], w3.rearrange("(k p) o -> p (k o)", p=P)).then_inc(w_in, 16)
                sp.dma_start(b1s[:, :], b1.rearrange("(k p) -> p k", p=P)).then_inc(w_in, 16)
                sp.dma_start(b2s[:, :], b2.rearrange("(k p) -> p k", p=P)).then_inc(w_in, 16)
            sp.wait_ge(l3_out, TILES)
            sp.dma_start(y.rearrange("b o -> o b"), ys[:, :]).then_inc(y_out, 16)
            sp.wait_ge(y_out, 16)

        @block.gpsimd
        def _(pool):
            pool.memset(ident[:, :], 0.0).then_inc(ident_zero, 1)
            pool.wait_ge(ident_zero, 1)
            pool.affine_select(out=ident[:, :], in_=ident[:, :], compare_op=ALU.not_equal, fill=1.0,
                               base=0, pattern=[[-1, P]], channel_multiplier=1).then_inc(ident_ready, 1)
            pool.wait_ge(idx_in, 16)
            for t in range(TILES):
                for f in range(TABLES):
                    pool.indirect_dma_start(emb[:, t, f, :], None, tables[f][:, :],
                                            bass.IndirectOffsetOnAxis(idx[:, t, f:f + 1], 0)
                                            ).then_inc(gathered[t][f // TGROUP], 16)

        def tp_copy(engine, copy, t, g):
            engine.wait_ge(tp_full, t * TGROUPS + g + 1)
            if t >= 2:
                engine.wait_ge(gram_full, GROUNDS * (t - 1))
            return copy(embT[:, t % 2, :, TGROUP * g:TGROUP * (g + 1)],
                        tp[g % 2][:, :, :].rearrange("p f b -> p b f"))

        def gram_copy(engine, copy, t, r, quadrants, done):
            n = t * GROUNDS + r
            engine.wait_ge(gram_full, n + 1)
            if t >= 2:
                engine.wait_ge(l1_full, t - 1)
            src = gram[n % 2]
            dst = zT[:, t % 2, :, :].rearrange("p c (q s) -> p s q c", s=QUADRANTS)
            for s in quadrants:
                for j in range(QUADRANTS):
                    m = CHUNKS if j < QUADRANTS - 1 else CHUNKS - 1
                    c0 = 32 * s + CHUNKS * j
                    last = copy(dst[32 * j:32 * j + 32, s, GQ * r:GQ * (r + 1), 0:m],
                                src[32 * s:32 * s + 32, :, c0:c0 + m])
            last.then_inc(done, 1)

        @block.vector
        def _(dve):
            nc.vector.memset(w1s[:, :, :], 0.0).then_inc(w1_zero, 1)
            nc.vector.memset(zT[96:128, :, CHUNKS - 1, :], 0.0).then_inc(z_zero, 1)
            for t in range(TILES):
                for g in range(0, TGROUPS, 2):
                    tp_copy(dve, nc.vector.tensor_copy, t, g).then_inc(tp_even_out, 1)
                dve.wait_ge(denT_full, t + 1)
                if t == 0:
                    dve.wait_ge(z_zero, 1)
                if t >= 2:
                    dve.wait_ge(l1_full, t - 1)
                nc.vector.tensor_copy(zT[96:96 + DENSE, t % 2, CHUNKS - 1, :], ps2[0:DENSE, 3, :]).then_inc(denT_out, 1)
                for r in range(GROUNDS):
                    gram_copy(dve, nc.vector.tensor_copy, t, r, (0, 1), gram_dve_out)
                if t == 0:
                    dve.wait_ge(w_in, 64)
                for hb in range(H1B):
                    dve.wait_ge(l1_full, t + 1)
                    last = nc.vector.tensor_scalar(h1[:, t % 2, hb, :], ps1[:, hb, :], b1s[:, hb:hb + 1], 0.0,
                                                   ALU.add, ALU.max)
                last.then_inc(l1_out, 1)
                dve.wait_ge(l2_full, t + 1)
                for ob in range(H2B):
                    last = nc.vector.tensor_scalar(h2[:, t % 2, ob, :], ps2[:, ob, :], b2s[:, ob:ob + 1], 0.0,
                                                   ALU.add, ALU.max)
                last.then_inc(l2_out, 1)
                dve.wait_ge(l3_full, t + 1)
                nc.vector.tensor_copy(ys[0:1, t * P:(t + 1) * P], ps2[0:1, 2, :]).then_inc(l3_out, 1)

        @block.scalar
        def _(act):
            for t in range(TILES):
                for g in range(1, TGROUPS, 2):
                    tp_copy(act, nc.scalar.copy, t, g).then_inc(tp_odd_out, 1)
                for r in range(GROUNDS):
                    gram_copy(act, nc.scalar.copy, t, r, (2, 3), gram_act_out)

        @block.tensor
        def _(pe):
            pe.wait_ge(ident_ready, 1)
            for t in range(TILES):
                for g in range(TGROUPS):
                    pe.wait_ge(gathered[t][g], 16 * TGROUP)
                    k = t * TGROUPS // 2 + g // 2
                    if k >= 1:
                        pe.wait_ge((tp_even_out, tp_odd_out)[g % 2], k)
                    for i in range(TGROUP):
                        last = nc.tensor.transpose(tp[g % 2][:, i, :], emb[:, t, TGROUP * g + i, :], ident[:, :])
                    last.then_inc(tp_full, 1)
                if t == 0:
                    pe.wait_ge(den_in, 16)
                if t >= 1:
                    pe.wait_ge(l3_out, t)
                nc.tensor.transpose(ps2[0:DENSE, 3, :], den[:, t, :], ident[:, :]).then_inc(denT_full, 1)
                pe.wait_ge(tp_even_out, (t + 1) * TGROUPS // 2)
                pe.wait_ge(tp_odd_out, (t + 1) * TGROUPS // 2)
                for r in range(GROUNDS):
                    n = t * GROUNDS + r
                    if n >= 2:
                        pe.wait_ge(gram_dve_out, n - 1)
                        pe.wait_ge(gram_act_out, n - 1)
                    for i in range(GQ):
                        q = GQ * r + i
                        quad = embT[:, t % 2, QUADRANTS * q:QUADRANTS * (q + 1), :].rearrange("p s f -> p (s f)")
                        last = nc.tensor.matmul(gram[n % 2][:, i, :], quad, quad, start=True, stop=True)
                    last.then_inc(gram_full, 1)
                if t == 0:
                    pe.wait_ge(w1_in, 16 * TABLES)
                    pe.wait_ge(w_in, 64)
                pe.wait_ge(denT_out, t + 1)
                pe.wait_ge(gram_dve_out, (t + 1) * GROUNDS)
                pe.wait_ge(gram_act_out, (t + 1) * GROUNDS)
                if t >= 1:
                    pe.wait_ge(l1_out, t)
                for hb in range(H1B):
                    for c in range(CHUNKS):
                        last = nc.tensor.matmul(ps1[:, hb, :], w1s[:, c, hb * P:(hb + 1) * P], zT[:, t % 2, c, :],
                                                start=(c == 0), stop=(c == CHUNKS - 1))
                last.then_inc(l1_full, 1)
                pe.wait_ge(l1_out, t + 1)
                for ob in range(H2B):
                    for hb in range(H1B):
                        last = nc.tensor.matmul(ps2[:, ob, :], w2s[:, hb, ob * P:(ob + 1) * P], h1[:, t % 2, hb, :],
                                                start=(hb == 0), stop=(hb == H1B - 1))
                last.then_inc(l2_full, 1)
                pe.wait_ge(l2_out, t + 1)
                for ob in range(H2B):
                    last = nc.tensor.matmul(ps2[0:1, 2, :], w3s[:, ob:ob + 1], h2[:, t % 2, ob, :],
                                            start=(ob == 0), stop=(ob == H2B - 1))
                last.then_inc(l3_full, 1)


_INS = (['dense_ctx', 'ids'] + [f'tbl_{f}' for f in range(TABLES)]
        + ['W_top1', 'b_top1', 'W_top2', 'b_top2', 'W_top3'])


def kernel(**inputs):
    import numpy as _np
    import concourse.bacc as _bacc
    from concourse import mybir as _mybir
    from concourse.bass_utils import run_bass_kernel_spmd as _run

    nc = _bacc.Bacc("TRN2", target_bir_lowering=False, num_devices=1)
    arrays, args = {}, {}
    for name in _INS:
        a = _np.ascontiguousarray(inputs[name])
        arrays[f"in_{name}"] = a
        args[name] = nc.dram_tensor(f"in_{name}", a.shape, _mybir.dt.from_np(a.dtype), kind="ExternalInput").ap()
    y = nc.dram_tensor("out_y", (BATCH, 1), _mybir.dt.float32, kind="ExternalOutput").ap()
    dlrm_tower(nc, args['dense_ctx'], args['ids'], [args[f'tbl_{f}'] for f in range(TABLES)],
               args['W_top1'], args['b_top1'], args['W_top2'], args['b_top2'], args['W_top3'], y)
    r = _run(nc, [arrays], core_ids=[0])
    return r.results[0]["out_y"]
```

```python
import concourse.bass as bass
from concourse import mybir
from contextlib import ExitStack

BATCH = 512
DIM = 128
DENSE = 16
P = 128
TILES = BATCH // P
QUADRANTS = 4
HID1, HID2 = 512, 256
H1B, H2B = HID1 // P, HID2 // P
QUADS = P // QUADRANTS
GQ = 8
GROUNDS = QUADS // GQ
TGROUP = 4
HALF = 16
SELECT_ROWS = 1000
MOST_SELECTED = 11


def feature_runs(features):
    runs = []
    for f in features:
        if runs and runs[-1][-1] == f - 1 and len(runs[-1]) < TGROUP:
            runs[-1].append(f)
        else:
            runs.append([f])
    return runs


def pair_row(a, b):
    return a * (2 * NF - a - 1) // 2 + b - a - 1


NF = 2 * HALF
SLOTS = HALF // QUADRANTS


def w1_pieces():
    pieces = []
    for m in range(HALF):
        j, c = m // SLOTS, m % SLOTS
        pieces.append((32 * j + m + 1, c, pair_row(m, m + 1), HALF - 1))
        if m < HALF - 1:
            pieces.append((32 * j + HALF + m + 1, c, pair_row(HALF + m, HALF + m + 1), HALF - 1 - m))
        for k in range(j, QUADRANTS):
            first = c if k == j else 0
            pieces.append((32 * k + m, first, pair_row(m, HALF + SLOTS * k + first), -(SLOTS - first)))
    return pieces


def dlrm_tower(nc, dense, ids, tables, w1, b1, w2, b2, w3, y):
    fp32 = mybir.dt.float32
    fp32r = mybir.dt.float32r
    i32 = mybir.dt.int32
    ACT = mybir.ActivationFunctionType
    ALU = mybir.AluOpType

    selected = [f for f in range(NF) if tables[f].shape[0] == SELECT_ROWS][:MOST_SELECTED]
    gathered = [f for f in range(NF) if f not in selected]
    S, G = len(selected), len(gathered)
    RP = 8
    RH = RP // 2
    TPART = SELECT_ROWS // RP
    assert TPART * RP == SELECT_ROWS and TPART <= P
    runs = feature_runs(gathered)
    NR = len(runs)
    OH = 4
    TB = 3
    pieces = w1_pieces()

    ctx = ExitStack()
    with ctx:
        def sb(name, shape, dt=fp32):
            return ctx.enter_context(nc.sbuf_tensor(name, shape, dt))

        def pb(name, shape):
            return ctx.enter_context(nc.psum_tensor(name, shape, fp32))

        def sem(name):
            return ctx.enter_context(nc.semaphore(name))

        idx = sb("idx", [P, TILES, NF], i32)
        idf = sb("idf", [P, TILES, NF])
        idT = sb("idT", [P, BATCH], fp32r)
        emb = sb("emb", [P, TILES, G, DIM])
        embT = sb("embT", [P, BATCH, NF])
        ident = sb("ident", [P, P])
        identr = sb("identr", [P, P], fp32r)
        zeros = sb("zeros", [P, 1])
        first_row = sb("first_row", [P, 1])
        gap = sb("gap", [P, HALF], i32)
        above = sb("above", [P, HALF], i32)
        mask = sb("mask", [P, HALF], i32)
        table = sb("table", [P, TB, RP, DIM])
        hi = sb("hi", [P, 2, RP, DIM], fp32r)
        lo = sb("lo", [P, 2, RP, DIM], fp32r)
        idb = sb("idb", [P, 2, BATCH])
        onehot = sb("onehot", [P, OH, BATCH], fp32r)
        den = sb("den", [P, TILES, DENSE])
        denT = sb("denT", [P, BATCH])
        w1s = sb("w1s", [P, SLOTS + 1, HID1])
        w2s = sb("w2s", [P, H1B, HID2])
        w3s = sb("w3s", [P, H2B])
        b1s = sb("b1s", [P, H1B])
        b2s = sb("b2s", [P, H2B])
        zT = sb("zT", [P, 2, SLOTS, P])
        h1 = sb("h1", [P, 2, H1B, P])
        h2 = sb("h2", [P, 2, H2B, P])
        ys = sb("ys", [1, BATCH])

        tp = [pb(f"tp{i}", [P, TGROUP, P]) for i in range(2)]
        gram = [pb(f"gram{i}", [P, GQ, P]) for i in range(2)]
        mlp = [pb(f"mlp{i}", [P, 4, P]) for i in range(2)]
        sel_ps = [gram[0][:, 4 * i:4 * i + 4, :].rearrange("p a b -> p (a b)") for i in range(2)]
        idb_ps = [gram[1][:, 4 * i:4 * i + 4, :].rearrange("p a b -> p (a b)") for i in range(2)]

        idx_in = sem("idx_in")
        rows_in = [[sem(f"rows_in_{t}_{g}") for g in range(NR)] for t in range(TILES)]
        table_in = [[sem(f"table_in_{i}_{h}") for h in range(2)] for i in range(TB)]
        zeros_ready = sem("zeros_ready")
        ident_zero = sem("ident_zero")
        ident_ready = sem("ident_ready")
        first_ready = sem("first_ready")
        gap_ready = sem("gap_ready")
        above_ready = sem("above_ready")
        mask_ready = sem("mask_ready")
        identr_ready = sem("identr_ready")
        idf_ready = sem("idf_ready")
        idT_zero = sem("idT_zero")
        idT_full = sem("idT_full")
        idT_ready = sem("idT_ready")
        denT_zero = sem("denT_zero")
        denT_full = sem("denT_full")
        denT_ready = sem("denT_ready")
        w1_zero_act = sem("w1_zero_act")
        w1_zero_dve = sem("w1_zero_dve")
        w1_in = sem("w1_in")
        w_in = sem("w_in")
        den_in = sem("den_in")
        hi_ready = sem("hi_ready")
        lo_ready = sem("lo_ready")
        idb_full = sem("idb_full")
        idb_ready = sem("idb_ready")
        onehot_ready = sem("onehot_ready")
        onehot_used = sem("onehot_used")
        sel_out = sem("sel_out")
        tp_full = sem("tp_full")
        tp_out = sem("tp_out")
        gram_full = sem("gram_full")
        gram_merged = sem("gram_merged")
        gram_dve_out = sem("gram_dve_out")
        gram_act_out = sem("gram_act_out")
        l1_full = sem("l1_full")
        l1_out = sem("l1_out")
        l2_full = sem("l2_full")
        l2_out = sem("l2_out")
        l3_full = sem("l3_full")
        l3_out = sem("l3_out")
        y_out = sem("y_out")
        block = ctx.enter_context(nc.Block())

        @block.sync
        def _(sp):
            def load_w1(piece):
                p, c, row, n = piece
                if n > 0:
                    dst, src = w1s[p:p + n, c, :], w1[row:row + n, :]
                else:
                    dst, src = w1s[p:p + 1, c:c - n, :], w1[row:row - n, :].rearrange("(a k) n -> a k n", a=1)
                sp.dma_start(dst, src).then_inc(w1_in, 16)

            sp.dma_start(idx[:, :, :], ids.rearrange("(t p) f -> p t f", p=P)).then_inc(idx_in, 16)
            per_turn = -(-len(pieces) // (S - TB))
            for x in range(S):
                if x >= TB:
                    sp.wait_ge(hi_ready, 2 * (x - TB + 1))
                    sp.wait_ge(lo_ready, 2 * (x - TB + 1))
                src = tables[selected[x]].rearrange("(p c) d -> p c d", c=RP)
                for h in range(2):
                    sp.dma_start(table[0:TPART, x % TB, RH * h:RH * (h + 1), :], src[:, RH * h:RH * (h + 1), :]
                                 ).then_inc(table_in[x % TB][h], 16)
                if x == 0:
                    sp.dma_start(den[:, :, :], dense.rearrange("(t p) f -> p t f", p=P)).then_inc(den_in, 16)
                if x == TB:
                    sp.wait_ge(w1_zero_act, 1)
                    sp.wait_ge(w1_zero_dve, 1)
                    row = pair_row(NF - 2, NF - 1) + 1
                    sp.dma_start(w1s[0:DENSE, SLOTS, :], w1[row:row + DENSE, :]).then_inc(w1_in, 16)
                if x >= TB:
                    for piece in pieces[per_turn * (x - TB):per_turn * (x - TB + 1)]:
                        load_w1(piece)
            sp.dma_start(w2s[:, :, :], w2.rearrange("(k p) n -> p k n", p=P)).then_inc(w_in, 16)
            with nc.allow_non_contiguous_dma(reason="short vectors"):
                sp.dma_start(w3s[:, :], w3.rearrange("(k p) o -> p (k o)", p=P)).then_inc(w_in, 16)
                sp.dma_start(b1s[:, :], b1.rearrange("(k p) -> p k", p=P)).then_inc(w_in, 16)
                sp.dma_start(b2s[:, :], b2.rearrange("(k p) -> p k", p=P)).then_inc(w_in, 16)
            sp.wait_ge(l3_out, TILES)
            sp.dma_start(y.rearrange("b o -> o b"), ys[:, :]).then_inc(y_out, 16)
            sp.wait_ge(y_out, 16)

        @block.gpsimd
        def _(pool):
            pool.memset(zeros[:, :], 0.0).then_inc(zeros_ready, 1)
            pool.memset(ident[:, :], 0.0).then_inc(ident_zero, 1)
            pool.wait_ge(ident_zero, 1)
            pool.affine_select(out=ident[:, :], in_=ident[:, :], compare_op=ALU.not_equal, fill=1.0,
                               base=0, pattern=[[-1, P]], channel_multiplier=1).then_inc(ident_ready, 1)
            pool.iota(first_row[:, :], pattern=[[0, 1]], base=0, channel_multiplier=-RP,
                      allow_small_or_imprecise_dtypes=True).then_inc(first_ready, 1)
            pool.wait_ge(first_ready, 1)
            for s in range(QUADRANTS):
                if s >= 1:
                    pool.wait_ge(gap_ready, s)
                pool.iota(gap[32 * s:32 * s + 32, :], pattern=[[-1, HALF]], base=0,
                          channel_multiplier=1).then_inc(gap_ready, 1)
            pool.wait_ge(idx_in, 16)
            for t in range(TILES):
                for g in range(NR):
                    for f in runs[g]:
                        pool.indirect_dma_start(emb[:, t, gathered.index(f), :], None, tables[f][:, :],
                                                bass.IndirectOffsetOnAxis(idx[:, t, f:f + 1], 0)
                                                ).then_inc(rows_in[t][g], 16)

        def gram_copy(engine, copy, t, r, quadrants, done):
            src = gram[(t * GROUNDS + r) % 2]
            dst = zT[:, t % 2, :, :].rearrange("p c (q s) -> p s q c", s=QUADRANTS)
            for s in quadrants:
                for j in range(QUADRANTS):
                    c0 = NF * s + HALF + SLOTS * j
                    last = copy(dst[32 * j:32 * j + 32, s, GQ * r:GQ * (r + 1), :],
                                src[32 * s:32 * s + 32, :, c0:c0 + SLOTS])
            last.then_inc(done, 1)

        @block.vector
        def _(dve):
            nc.vector.memset(w1s[:, 0:2, :], 0.0).then_inc(w1_zero_dve, 1)
            nc.vector.memset(idT[:, :].bitcast(fp32), 0.0).then_inc(idT_zero, 1)
            dve.wait_ge(idx_in, 16)
            nc.vector.tensor_copy(idf[:, :, :], idx[:, :, :]).then_inc(idf_ready, 1)
            dve.wait_ge(ident_ready, 1)
            nc.vector.tensor_copy(identr[:, :], ident[:, :]).then_inc(identr_ready, 1)
            nc.vector.memset(denT[:, :], 0.0).then_inc(denT_zero, 1)
            dve.wait_ge(gap_ready, QUADRANTS)
            nc.vector.tensor_scalar(above[:, :], gap[:, :], 1.0, None, ALU.is_ge).then_inc(above_ready, 1)
            dve.wait_ge(above_ready, 1)
            nc.vector.scalar_tensor_tensor(out=mask[:, :], in0=gap[:, :], scalar=float(HALF - 1), in1=above[:, :],
                                           op0=ALU.is_le, op1=ALU.mult).then_inc(mask_ready, 1)

            def split_lo(x, h):
                dve.wait_ge(hi_ready, 2 * x + h + 1)
                if x >= 2:
                    dve.wait_ge(onehot_used, RP * (x - 1))
                part = slice(RH * h, RH * (h + 1))
                nc.vector.tensor_tensor(lo[0:TPART, x % 2, part, :], table[0:TPART, x % TB, part, :],
                                        hi[0:TPART, x % 2, part, :].bitcast(fp32), ALU.subtract
                                        ).then_inc(lo_ready, 1)

            def make_onehot(x, c):
                k = x * RP + c
                if k >= OH:
                    dve.wait_ge(onehot_used, k - OH + 1)
                nc.vector.tensor_scalar(onehot[0:TPART, k % OH, :], idb[0:TPART, x % 2, :], float(c), None,
                                        ALU.is_equal).then_inc(onehot_ready, 1)

            for x in range(S):
                split_lo(x, 0)
                dve.wait_ge(idb_ready, x + 1)
                for c in range(RH):
                    make_onehot(x, c)
                split_lo(x, 1)
                for c in range(RH, RP):
                    make_onehot(x, c)
                if x == 0:
                    dve.wait_ge(denT_full, 1)
                    dve.wait_ge(denT_zero, 1)
                    nc.vector.tensor_copy(denT[0:DENSE, :],
                                          mlp[1][0:DENSE, :, :].rearrange("p a b -> p (a b)")).then_inc(denT_ready, 1)
            dve.wait_ge(mask_ready, 1)
            for t in range(TILES):
                for r in range(GROUNDS):
                    n = t * GROUNDS + r
                    dve.wait_ge(gram_full, n + 1)
                    blocks = gram[n % 2][:, :, :].rearrange("p q (s f) -> p (q s) f", s=QUADRANTS)
                    nc.vector.copy_predicated(blocks[:, :, HALF:NF],
                                              mask[:, :].unsqueeze(1).broadcast_to([P, GQ * QUADRANTS, HALF]),
                                              blocks[:, :, 0:HALF]).then_inc(gram_merged, 1)
                    dve.wait_ge(gram_merged, n + 1)
                    if t >= 2:
                        dve.wait_ge(l1_full, 2 * (t - 1))
                    gram_copy(dve, nc.vector.tensor_copy, t, r, (0, 1), gram_dve_out)
                if t == 0:
                    dve.wait_ge(w_in, 64)
                for hb in range(H1B):
                    dve.wait_ge(l1_full, 2 * t + hb // 2 + 1)
                    nc.vector.tensor_scalar(h1[:, t % 2, hb, :], mlp[hb // 2][:, hb % 2, :], b1s[:, hb:hb + 1], 0.0,
                                            ALU.add, ALU.max).then_inc(l1_out, 1)
                for ob in range(H2B):
                    dve.wait_ge(l2_full, H2B * t + ob + 1)
                    nc.vector.tensor_scalar(h2[:, t % 2, ob, :], mlp[ob][:, 2, :], b2s[:, ob:ob + 1], 0.0,
                                            ALU.add, ALU.max).then_inc(l2_out, 1)
                dve.wait_ge(l3_full, t + 1)
                nc.vector.tensor_copy(ys[0:1, t * P:(t + 1) * P], mlp[0][0:1, 3, :]).then_inc(l3_out, 1)

        def early_runs(x):
            return [x - 1] if 1 <= x <= NR else []

        @block.scalar
        def _(act):
            def tp_copy(t, g):
                act.wait_ge(tp_full, t * NR + g + 1)
                n, f = len(runs[g]), runs[g][0]
                nc.scalar.copy(embT[:, t * P:(t + 1) * P, f:f + n],
                               tp[g % 2][:, 0:n, :].rearrange("p f b -> p b f")).then_inc(tp_out, 1)

            def split_hi(x, h):
                act.wait_ge(table_in[x % TB][h], 16 * (x // TB + 1))
                if x >= 2:
                    act.wait_ge(onehot_used, RP * (x - 1))
                part = slice(RH * h, RH * (h + 1))
                nc.scalar.copy(hi[0:TPART, x % 2, part, :], table[0:TPART, x % TB, part, :]).then_inc(hi_ready, 1)

            def spread_ids(x):
                act.wait_ge(idb_full, x + 1)
                if x >= 2:
                    act.wait_ge(onehot_ready, RP * (x - 1))
                nc.scalar.activation(idb[:, x % 2, :], idb_ps[x % 2], ACT.Identity,
                                     bias=first_row[:, 0:1]).then_inc(idb_ready, 1)

            act.wait_ge(zeros_ready, 1)
            n = SLOTS - 1
            nc.scalar.activation(w1s[:, 2:SLOTS + 1, :].rearrange("p c n -> p (c n)"),
                                 zeros[:, 0:1].broadcast_to([P, n * HID1]), ACT.Identity).then_inc(w1_zero_act, 1)
            split_hi(0, 0)
            act.wait_ge(idT_zero, 1)
            act.wait_ge(idT_full, 1)
            nc.scalar.copy(idT[0:NF, :], mlp[0][0:NF, :, :].rearrange("p a b -> p (a b)")).then_inc(idT_ready, 1)
            split_hi(0, 1)
            act.wait_ge(first_ready, 1)
            spread_ids(0)
            for x in range(S):
                if x + 1 < S:
                    spread_ids(x + 1)
                    split_hi(x + 1, 0)
                    split_hi(x + 1, 1)
                for g in early_runs(x):
                    tp_copy(0, g)
                act.wait_ge(onehot_used, RP * (x + 1))
                nc.scalar.copy(embT[:, :, selected[x]], sel_ps[x % 2]).then_inc(sel_out, 1)
            for t in range(TILES):
                if t == 0:
                    for g in range(S - 1, NR):
                        tp_copy(0, g)
                for r in range(GROUNDS):
                    act.wait_ge(gram_merged, t * GROUNDS + r + 1)
                    if t >= 2:
                        act.wait_ge(l1_full, 2 * (t - 1))
                    gram_copy(act, nc.scalar.copy, t, r, (2, 3), gram_act_out)
                if t + 1 < TILES:
                    for g in range(NR):
                        tp_copy(t + 1, g)

        @block.tensor
        def _(pe):
            def transposes(t, g):
                pe.wait_ge(rows_in[t][g], 16 * len(runs[g]))
                k = t * NR + g
                if k >= 2:
                    pe.wait_ge(tp_out, k - 1)
                for i, f in enumerate(runs[g]):
                    last = nc.tensor.transpose(tp[g % 2][:, i, :], emb[:, t, gathered.index(f), :], ident[:, :])
                last.then_inc(tp_full, 1)

            def broadcast_ids(x):
                if x >= 2:
                    pe.wait_ge(idb_ready, x - 1)
                f = selected[x]
                nc.tensor.matmul(idb_ps[x % 2], identr[:, f:f + 1].broadcast_to([P, P]), idT[:, :],
                                 start=True, stop=True).then_inc(idb_full, 1)

            pe.wait_ge(ident_ready, 1)
            pe.wait_ge(idf_ready, 1)
            for t in range(TILES):
                last = nc.tensor.transpose(mlp[0][0:NF, t, :], idf[:, t, :], ident[:, :])
            last.then_inc(idT_full, 1)
            pe.wait_ge(den_in, 16)
            for t in range(TILES):
                last = nc.tensor.transpose(mlp[1][0:DENSE, t, :], den[:, t, :], ident[:, :])
            last.then_inc(denT_full, 1)
            pe.wait_ge(identr_ready, 1)
            pe.wait_ge(idT_ready, 1)
            broadcast_ids(0)
            for x in range(S):
                if x + 1 < S:
                    broadcast_ids(x + 1)
                if x >= 2:
                    pe.wait_ge(sel_out, x - 1)
                for c in range(RP):
                    k = x * RP + c
                    if c % RH == 0:
                        pe.wait_ge(hi_ready, 2 * x + c // RH + 1)
                        pe.wait_ge(lo_ready, 2 * x + c // RH + 1)
                    pe.wait_ge(onehot_ready, k + 1)
                    nc.tensor.matmul(sel_ps[x % 2], hi[0:TPART, x % 2, c, :], onehot[0:TPART, k % OH, :],
                                     start=(c == 0), stop=False)
                    nc.tensor.matmul(sel_ps[x % 2], lo[0:TPART, x % 2, c, :], onehot[0:TPART, k % OH, :],
                                     start=False, stop=(c == RP - 1)).then_inc(onehot_used, 1)
                for g in early_runs(x):
                    transposes(0, g)
            for g in range(S - 1, NR):
                transposes(0, g)
            for t in range(TILES):
                ahead = list(range(NR)) if t + 1 < TILES else []

                def fill(n):
                    for _ in range(min(n, len(ahead))):
                        transposes(t + 1, ahead.pop(0))

                pe.wait_ge(tp_out, (t + 1) * NR)
                pe.wait_ge(sel_out, S)
                for r in range(GROUNDS):
                    n = t * GROUNDS + r
                    if n >= 2:
                        pe.wait_ge(gram_dve_out, n - 1)
                        pe.wait_ge(gram_act_out, n - 1)
                    for i in range(GQ):
                        b = t * P + QUADRANTS * (GQ * r + i)
                        quad = embT[:, b:b + QUADRANTS, :].rearrange("p s f -> p (s f)")
                        last = nc.tensor.matmul(gram[n % 2][:, i, :], quad, quad, start=True, stop=True)
                    last.then_inc(gram_full, 1)
                fill(2)
                if t == 0:
                    pe.wait_ge(w1_in, 16 * (len(pieces) + 1))
                    pe.wait_ge(w_in, 64)
                    pe.wait_ge(denT_ready, 1)
                if t >= 1:
                    pe.wait_ge(l3_out, t)

                def layer1(hb, c, start):
                    rhs = denT[:, t * P:(t + 1) * P] if c == SLOTS else zT[:, t % 2, c, :]
                    return nc.tensor.matmul(mlp[hb // 2][:, hb % 2, :], w1s[:, c, hb * P:(hb + 1) * P], rhs,
                                            start=start, stop=(c == SLOTS - 1), skip_group_check=True)

                for hb in range(H1B):
                    layer1(hb, SLOTS, hb % 2 == 0)
                pe.wait_ge(gram_dve_out, (t + 1) * GROUNDS)
                pe.wait_ge(gram_act_out, (t + 1) * GROUNDS)
                for hb in range(H1B):
                    for c in range(SLOTS):
                        last = layer1(hb, c, False)
                    if hb % 2:
                        last.then_inc(l1_full, 1)
                        fill(2)
                for ob in range(H2B):
                    for hb in range(H1B):
                        if ob == 0:
                            pe.wait_ge(l1_out, H1B * t + max(hb + 1, 2))
                        last = nc.tensor.matmul(mlp[ob][:, 2, :], w2s[:, hb, ob * P:(ob + 1) * P], h1[:, t % 2, hb, :],
                                                start=(hb == 0), stop=(hb == H1B - 1))
                    last.then_inc(l2_full, 1)
                fill(NR)
                for ob in range(H2B):
                    pe.wait_ge(l2_out, H2B * t + ob + 1)
                    last = nc.tensor.matmul(mlp[0][0:1, 3, :], w3s[:, ob:ob + 1], h2[:, t % 2, ob, :],
                                            start=(ob == 0), stop=(ob == H2B - 1))
                last.then_inc(l3_full, 1)


_INS = (['dense_ctx', 'ids'] + [f'tbl_{f}' for f in range(32)]
        + ['W_top1', 'b_top1', 'W_top2', 'b_top2', 'W_top3'])


def kernel(**inputs):
    import numpy as _np
    import concourse.bacc as _bacc
    from concourse import mybir as _mybir
    from concourse.bass_utils import run_bass_kernel_spmd as _run

    nc = _bacc.Bacc("TRN2", target_bir_lowering=False, num_devices=1)
    arrays, args = {}, {}
    for name in _INS:
        a = _np.ascontiguousarray(inputs[name])
        arrays[f"in_{name}"] = a
        args[name] = nc.dram_tensor(f"in_{name}", a.shape, _mybir.dt.from_np(a.dtype), kind="ExternalInput").ap()
    y = nc.dram_tensor("out_y", (BATCH, 1), _mybir.dt.float32, kind="ExternalOutput").ap()
    dlrm_tower(nc, args['dense_ctx'], args['ids'], [args[f'tbl_{f}'] for f in range(32)],
               args['W_top1'], args['b_top1'], args['W_top2'], args['b_top2'], args['W_top3'], y)
    r = _run(nc, [arrays], core_ids=[0])
    return r.results[0]["out_y"]
```

```python
import concourse.bass as bass
from concourse import mybir
from contextlib import ExitStack

BATCH = 512
DIM = 128
DENSE = 16
P = 128
TILES = BATCH // P
QUADRANTS = 4
HID1, HID2 = 512, 256
H1B, H2B = HID1 // P, HID2 // P
QUADS = P // QUADRANTS
GQ = 8
GROUNDS = QUADS // GQ
TGROUP = 4
HALF = 16
SELECT_ROWS = 1000
MOST_SELECTED = 11


def feature_runs(features):
    runs = []
    for f in features:
        if runs and runs[-1][-1] == f - 1 and len(runs[-1]) < TGROUP:
            runs[-1].append(f)
        else:
            runs.append([f])
    return runs


def pair_row(a, b):
    return a * (2 * NF - a - 1) // 2 + b - a - 1


NF = 2 * HALF
SLOTS = HALF // QUADRANTS


def w1_pieces():
    pieces = []
    for m in range(HALF):
        j, c = m // SLOTS, m % SLOTS
        pieces.append((32 * j + m + 1, 1, HALF - 1, c, 1, pair_row(m, m + 1)))
        if m < HALF - 1:
            pieces.append((32 * j + HALF + m + 1, 1, HALF - 1 - m, c, 1, pair_row(HALF + m, HALF + m + 1)))
        pieces.append((32 * j + m, 32, 1, c, SLOTS - c, pair_row(m, HALF + m)))
        if j < QUADRANTS - 1:
            pieces.append((32 * (j + 1) + m, 32, QUADRANTS - 1 - j, 0, SLOTS, pair_row(m, HALF + SLOTS * (j + 1))))
    return pieces


def dlrm_tower(nc, dense, ids, tables, w1, b1, w2, b2, w3, y):
    fp32 = mybir.dt.float32
    fp32r = mybir.dt.float32r
    i32 = mybir.dt.int32
    ACT = mybir.ActivationFunctionType
    ALU = mybir.AluOpType

    selected = [f for f in range(NF) if tables[f].shape[0] == SELECT_ROWS][:MOST_SELECTED]
    gathered = [f for f in range(NF) if f not in selected]
    S, G = len(selected), len(gathered)
    RP = 8
    RH = RP // 2
    TPART = SELECT_ROWS // RP
    assert TPART * RP == SELECT_ROWS and TPART <= P
    runs = feature_runs(gathered)
    NR = len(runs)
    OH = 4
    TB = 3
    pieces = w1_pieces()

    ctx = ExitStack()
    with ctx:
        def sb(name, shape, dt=fp32):
            return ctx.enter_context(nc.sbuf_tensor(name, shape, dt))

        def pb(name, shape):
            return ctx.enter_context(nc.psum_tensor(name, shape, fp32))

        def sem(name):
            return ctx.enter_context(nc.semaphore(name))

        idx = sb("idx", [P, TILES, NF], i32)
        idf = sb("idf", [P, TILES, NF])
        idr = sb("idr", [P, TILES, NF], fp32r)
        idT = sb("idT", [P, BATCH], fp32r)
        emb = sb("emb", [P, TILES, G, DIM])
        embT = sb("embT", [P, BATCH, NF])
        ident = sb("ident", [P, P])
        identr = sb("identr", [P, P], fp32r)
        zeros = sb("zeros", [P, 1])
        first_row = sb("first_row", [P, 1])
        gap = sb("gap", [P, HALF], i32)
        above = sb("above", [P, HALF], i32)
        mask = sb("mask", [P, HALF], i32)
        table = sb("table", [P, TB, RP, DIM])
        hi = sb("hi", [P, 2, RP, DIM], fp32r)
        lo = sb("lo", [P, 2, RP, DIM], fp32r)
        idb = sb("idb", [P, 2, BATCH])
        onehot = sb("onehot", [P, OH, BATCH], fp32r)
        den = sb("den", [P, TILES, DENSE])
        den32 = sb("den32", [DENSE, BATCH])
        w1den = sb("w1den", [DENSE, HID1])
        den_parts = sb("den_parts", [P, BATCH], fp32r)
        w1den_parts = sb("w1den_parts", [P, HID1], fp32r)
        w1s = sb("w1s", [P, SLOTS, HID1])
        w2s = sb("w2s", [P, H1B, HID2])
        w3s = sb("w3s", [P, H2B])
        b1s = sb("b1s", [P, H1B])
        b2s = sb("b2s", [P, H2B])
        zT = sb("zT", [P, SLOTS, BATCH])
        h1 = sb("h1", [P, H1B, BATCH])
        h2 = sb("h2", [P, H2B, BATCH])
        ys = sb("ys", [1, BATCH])

        tp = [pb(f"tp{i}", [P, TGROUP, P]) for i in range(2)]
        gram = [pb(f"gram{i}", [P, GQ, P]) for i in range(2)]
        mlp = [pb(f"mlp{i}", [P, 4, P]) for i in range(2)]

        def bank(tensor, half=0):
            return tensor[:, 4 * half:4 * half + 4, :].rearrange("p a b -> p (a b)")

        EARLY, LATE = 0, 1
        GROUPS = [(0, (TILES - 1) * P), ((TILES - 1) * P, BATCH)]
        L1_BANKS = [[bank(mlp[0]), bank(mlp[1]), bank(gram[0], 0), bank(gram[0], 1)],
                    [bank(tp[0]), bank(gram[0], 0), bank(gram[0], 1), bank(tp[1])]]
        L2_BANKS = [bank(mlp[0]), bank(mlp[1])]
        L2_PARTS = [((0, 1), (0, 1)), ((0,), (2,)), ((1,), (2,)), ((0,), (3,)), ((1,), (3,))]
        L3_BANK = [bank(tp[1]), bank(gram[1], 0)]
        sel_ps = [bank(gram[0], i) for i in range(2)]
        idb_ps = [bank(gram[1], i) for i in range(2)]

        idx_in = sem("idx_in")
        rows_in = [[sem(f"rows_in_{t}_{g}") for g in range(NR)] for t in range(TILES)]
        table_in = [[sem(f"table_in_{i}_{h}") for h in range(2)] for i in range(TB)]
        zeros_ready = sem("zeros_ready")
        ident_zero = sem("ident_zero")
        ident_ready = sem("ident_ready")
        first_ready = sem("first_ready")
        gap_ready = sem("gap_ready")
        above_ready = sem("above_ready")
        mask_ready = sem("mask_ready")
        identr_ready = sem("identr_ready")
        idf_ready = sem("idf_ready")
        idT_zero = sem("idT_zero")
        idT_full = sem("idT_full")
        idT_ready = sem("idT_ready")
        parts_zero = sem("parts_zero")
        denT_full = sem("denT_full")
        den32_ready = sem("den32_ready")
        den_hi_ready = sem("den_hi_ready")
        den_lo_ready = sem("den_lo_ready")
        w1den_in = sem("w1den_in")
        w1_zero_act = sem("w1_zero_act")
        w1_zero_dve = sem("w1_zero_dve")
        w1_in = sem("w1_in")
        w_in = sem("w_in")
        den_in = sem("den_in")
        hi_ready = sem("hi_ready")
        lo_ready = sem("lo_ready")
        idb_full = sem("idb_full")
        idb_ready = sem("idb_ready")
        onehot_ready = sem("onehot_ready")
        onehot_used = sem("onehot_used")
        sel_out = sem("sel_out")
        tp_full = sem("tp_full")
        tp_out = sem("tp_out")
        gram_full = sem("gram_full")
        gram_merged = sem("gram_merged")
        gram_dve_out = sem("gram_dve_out")
        gram_act_out = sem("gram_act_out")
        l1_full = sem("l1_full")
        l1_out = sem("l1_out")
        l2_full = sem("l2_full")
        l2_out = sem("l2_out")
        l3_full = sem("l3_full")
        l3_out = sem("l3_out")
        y_out = sem("y_out")
        block = ctx.enter_context(nc.Block())

        def steps(kind, t, parts):
            return [(kind, t, part) for part in parts]

        STEPS = (steps("transposes", 1, (0, 1))
                 + steps("gram", 0, (0,)) + steps("transposes", 1, (2, 3))
                 + steps("gram", 0, (1,)) + steps("transposes", 1, (4, 5))
                 + steps("gram", 0, (2,)) + steps("transposes", 1, (6, 7)) + steps("gram", 0, (3,))
                 + steps("gram", 1, (0,)) + steps("transposes", 2, (0,))
                 + steps("gram", 1, (1,)) + steps("transposes", 2, (1,))
                 + steps("gram", 1, (2,)) + steps("transposes", 2, (2,))
                 + steps("gram", 1, (3,)) + steps("transposes", 2, (3, 4))
                 + steps("layer1", 0, (0, 1)) + steps("transposes", 2, (5,)) + steps("layer1", 1, (0,))
                 + steps("transposes", 2, (6, 7)) + steps("layer1", 1, (1,))
                 + steps("gram", 2, (0, 1)) + steps("transposes", 3, (0,))
                 + steps("gram", 2, (2, 3)) + steps("transposes", 3, (1,))
                 + steps("layer1", 0, (2, 3)) + steps("transposes", 3, (2,))
                 + steps("layer1", 1, (2, 3)) + steps("transposes", 3, (3,))
                 + steps("layer1", 2, (0, 1, 2)) + steps("transposes", 3, (4,))
                 + steps("layer1", 2, (3,)) + steps("transposes", 3, (5,))
                 + steps("layer2", EARLY, (0,)) + steps("transposes", 3, (6, 7)) + steps("layer2", EARLY, (1,))
                 + steps("gram", 3, range(GROUNDS))
                 + steps("layer2", EARLY, (2, 3, 4))
                 + steps("layer1", 3, (0,)) + steps("layer3", EARLY, (0,)) + steps("layer1", 3, (1, 2, 3))
                 + steps("layer2", LATE, range(len(L2_PARTS))) + steps("layer3", LATE, (0,)))
        assert [g for kind, t, g in STEPS if kind == "transposes" and t == 3] == list(range(NR))

        @block.sync
        def _(sp):
            def load_w1(piece):
                p, step, n, c, m, row = piece
                sp.dma_start(w1s[p:p + step * (n - 1) + 1:step, c:c + m, :],
                             w1[row:row + n * m, :].rearrange("(a k) n -> a k n", k=m)).then_inc(w1_in, 16)

            sp.dma_start(idx[:, :, :], ids.rearrange("(t p) f -> p t f", p=P)).then_inc(idx_in, 16)
            per_turn = 5
            for x in range(S):
                if x >= TB:
                    sp.wait_ge(hi_ready, 2 * (x - TB + 1))
                    sp.wait_ge(lo_ready, 2 * (x - TB + 1))
                src = tables[selected[x]].rearrange("(p c) d -> p c d", c=RP)
                for h in range(2):
                    sp.dma_start(table[0:TPART, x % TB, RH * h:RH * (h + 1), :], src[:, RH * h:RH * (h + 1), :]
                                 ).then_inc(table_in[x % TB][h], 16)
                if x == 0:
                    sp.dma_start(den[:, :, :], dense.rearrange("(t p) f -> p t f", p=P)).then_inc(den_in, 16)
                    row = pair_row(NF - 2, NF - 1) + 1
                    sp.dma_start(w1den[0:DENSE, :], w1[row:row + DENSE, :]).then_inc(w1den_in, 16)
                if x == TB:
                    sp.wait_ge(w1_zero_act, 1)
                    sp.wait_ge(w1_zero_dve, 1)
                if x >= TB:
                    for piece in pieces[per_turn * (x - TB):per_turn * (x - TB + 1)]:
                        load_w1(piece)
            for piece in pieces[per_turn * (S - TB):]:
                load_w1(piece)
            sp.dma_start(w2s[:, :, :], w2.rearrange("(k p) n -> p k n", p=P)).then_inc(w_in, 16)
            with nc.allow_non_contiguous_dma(reason="short vectors"):
                sp.dma_start(w3s[:, :], w3.rearrange("(k p) o -> p (k o)", p=P)).then_inc(w_in, 16)
                sp.dma_start(b1s[:, :], b1.rearrange("(k p) -> p k", p=P)).then_inc(w_in, 16)
                sp.dma_start(b2s[:, :], b2.rearrange("(k p) -> p k", p=P)).then_inc(w_in, 16)
            sp.wait_ge(l3_out, len(GROUPS))
            sp.dma_start(y.rearrange("b o -> o b"), ys[:, :]).then_inc(y_out, 16)
            sp.wait_ge(y_out, 16)

        @block.gpsimd
        def _(pool):
            pool.memset(zeros[:, :], 0.0).then_inc(zeros_ready, 1)
            pool.memset(ident[:, :], 0.0).then_inc(ident_zero, 1)
            pool.wait_ge(ident_zero, 1)
            pool.affine_select(out=ident[:, :], in_=ident[:, :], compare_op=ALU.not_equal, fill=1.0,
                               base=0, pattern=[[-1, P]], channel_multiplier=1).then_inc(ident_ready, 1)
            pool.iota(first_row[:, :], pattern=[[0, 1]], base=0, channel_multiplier=-RP,
                      allow_small_or_imprecise_dtypes=True).then_inc(first_ready, 1)
            pool.wait_ge(first_ready, 1)
            for s in range(QUADRANTS):
                if s >= 1:
                    pool.wait_ge(gap_ready, s)
                pool.iota(gap[32 * s:32 * s + 32, :], pattern=[[-1, HALF]], base=0,
                          channel_multiplier=1).then_inc(gap_ready, 1)
            pool.wait_ge(idx_in, 16)
            for t in range(TILES):
                for g in range(NR):
                    for f in runs[g]:
                        pool.indirect_dma_start(emb[:, t, gathered.index(f), :], None, tables[f][:, :],
                                                bass.IndirectOffsetOnAxis(idx[:, t, f:f + 1], 0)
                                                ).then_inc(rows_in[t][g], 16)

        def gram_copy(engine, copy, t, r, quadrants, done):
            src = gram[(t * GROUNDS + r) % 2]
            dst = zT[:, :, t * P:(t + 1) * P].rearrange("p c (q s) -> p s q c", s=QUADRANTS)
            for s in quadrants:
                for j in range(QUADRANTS):
                    c0 = NF * s + HALF + SLOTS * j
                    last = copy(dst[32 * j:32 * j + 32, s, GQ * r:GQ * (r + 1), :],
                                src[32 * s:32 * s + 32, :, c0:c0 + SLOTS])
            last.then_inc(done, 1)

        @block.vector
        def _(dve):
            nc.vector.memset(w1s[:, 0:2, :], 0.0).then_inc(w1_zero_dve, 1)
            nc.vector.memset(idT[:, :].bitcast(fp32), 0.0).then_inc(idT_zero, 1)
            nc.vector.memset(den_parts[:, :].bitcast(fp32), 0.0).then_inc(parts_zero, 1)
            dve.wait_ge(idx_in, 16)
            nc.vector.tensor_copy(idr[:, :, :], idx[:, :, :]).then_inc(idf_ready, 1)
            nc.vector.tensor_copy(idf[:, :, :], idx[:, :, :]).then_inc(idf_ready, 1)
            dve.wait_ge(ident_ready, 1)
            nc.vector.tensor_copy(identr[:, :], ident[:, :]).then_inc(identr_ready, 1)
            dve.wait_ge(gap_ready, QUADRANTS)
            nc.vector.tensor_scalar(above[:, :], gap[:, :], 1.0, None, ALU.is_ge).then_inc(above_ready, 1)
            dve.wait_ge(above_ready, 1)
            nc.vector.scalar_tensor_tensor(out=mask[:, :], in0=gap[:, :], scalar=float(HALF - 1), in1=above[:, :],
                                           op0=ALU.is_le, op1=ALU.mult).then_inc(mask_ready, 1)

            def split_lo(x, h):
                dve.wait_ge(hi_ready, 2 * x + h + 1)
                if x >= 2:
                    dve.wait_ge(onehot_used, RP * (x - 1))
                part = slice(RH * h, RH * (h + 1))
                nc.vector.tensor_tensor(lo[0:TPART, x % 2, part, :], table[0:TPART, x % TB, part, :],
                                        hi[0:TPART, x % 2, part, :].bitcast(fp32), ALU.subtract
                                        ).then_inc(lo_ready, 1)

            def make_onehot(x, c):
                k = x * RP + c
                if k >= OH:
                    dve.wait_ge(onehot_used, k - OH + 1)
                nc.vector.tensor_scalar(onehot[0:TPART, k % OH, :], idb[0:TPART, x % 2, :], float(c), None,
                                        ALU.is_equal).then_inc(onehot_ready, 1)

            def split_dense_lo():
                dve.wait_ge(den_hi_ready, 4)
                for q in (2, 3):
                    nc.vector.tensor_tensor(den_parts[32 * q:32 * q + DENSE, :], den32[:, :],
                                            den_parts[0:DENSE, :].bitcast(fp32), ALU.subtract
                                            ).then_inc(den_lo_ready, 1)
                for q in (1, 3):
                    nc.vector.tensor_tensor(w1den_parts[32 * q:32 * q + DENSE, :], w1den[:, :],
                                            w1den_parts[0:DENSE, :].bitcast(fp32), ALU.subtract
                                            ).then_inc(den_lo_ready, 1)

            for x in range(S):
                split_lo(x, 0)
                dve.wait_ge(idb_ready, x + 1)
                for c in range(RH):
                    make_onehot(x, c)
                split_lo(x, 1)
                for c in range(RH, RP):
                    make_onehot(x, c)
            dve.wait_ge(mask_ready, 1)

            def take_gram(t, r):
                n = t * GROUNDS + r
                dve.wait_ge(gram_full, n + 1)
                blocks = gram[n % 2][:, :, :].rearrange("p q (s f) -> p (q s) f", s=QUADRANTS)
                nc.vector.copy_predicated(blocks[:, :, HALF:NF],
                                          mask[:, :].unsqueeze(1).broadcast_to([P, GQ * QUADRANTS, HALF]),
                                          blocks[:, :, 0:HALF]).then_inc(gram_merged, 1)
                dve.wait_ge(gram_merged, n + 1)
                gram_copy(dve, nc.vector.tensor_copy, t, r, (0, 1), gram_dve_out)

            def take_layer1(t, hb):
                if t + 1 < TILES - 1:
                    return
                group = t // (TILES - 1)
                if group == EARLY and hb == 0:
                    dve.wait_ge(w_in, 64)
                b0, b1 = GROUPS[group]
                dve.wait_ge(l1_full, H1B * group + hb + 1)
                nc.vector.tensor_scalar(h1[:, hb, b0:b1], L1_BANKS[group][hb][:, 0:b1 - b0],
                                        b1s[:, hb:hb + 1], 0.0, ALU.add, ALU.max).then_inc(l1_out, 1)

            def take_layer3(group, _):
                b0, b1 = GROUPS[group]
                dve.wait_ge(l3_full, group + 1)
                nc.vector.tensor_copy(ys[0:1, b0:b1], L3_BANK[group][0:1, 0:b1 - b0]).then_inc(l3_out, 1)

            split_dense_lo()
            take = {"gram": take_gram, "layer1": take_layer1, "layer3": take_layer3}
            for kind, t, part in STEPS:
                if kind in take:
                    take[kind](t, part)

        def early_runs(x):
            return [x - 1] if 1 <= x <= NR else []

        @block.scalar
        def _(act):
            def tp_copy(t, g):
                act.wait_ge(tp_full, t * NR + g + 1)
                n, f = len(runs[g]), runs[g][0]
                nc.scalar.copy(embT[:, t * P:(t + 1) * P, f:f + n],
                               tp[g % 2][:, 0:n, :].rearrange("p f b -> p b f")).then_inc(tp_out, 1)

            def split_hi(x, h):
                act.wait_ge(table_in[x % TB][h], 16 * (x // TB + 1))
                if x >= 2:
                    act.wait_ge(onehot_used, RP * (x - 1))
                part = slice(RH * h, RH * (h + 1))
                nc.scalar.copy(hi[0:TPART, x % 2, part, :], table[0:TPART, x % TB, part, :]).then_inc(hi_ready, 1)

            def spread_ids(x):
                act.wait_ge(idb_full, x + 1)
                if x >= 2:
                    act.wait_ge(onehot_ready, RP * (x - 1))
                nc.scalar.activation(idb[:, x % 2, :], idb_ps[x % 2], ACT.Identity,
                                     bias=first_row[:, 0:1]).then_inc(idb_ready, 1)

            act.wait_ge(zeros_ready, 1)
            nc.scalar.activation(w1s[:, 2:SLOTS, :].rearrange("p c n -> p (c n)"),
                                 zeros[:, 0:1].broadcast_to([P, 2 * HID1]), ACT.Identity).then_inc(w1_zero_act, 1)
            nc.scalar.activation(w1den_parts[:, :], zeros[:, 0:1].broadcast_to([P, HID1]), ACT.Identity
                                 ).then_inc(parts_zero, 1)
            split_hi(0, 0)
            act.wait_ge(first_ready, 1)
            spread_ids(0)
            split_hi(0, 1)
            act.wait_ge(idT_zero, 1)
            act.wait_ge(idT_full, 1)
            nc.scalar.copy(idT[0:NF, :], mlp[0][0:NF, :, :].rearrange("p a b -> p (a b)")).then_inc(idT_ready, 1)
            for x in range(S):
                if x + 1 < S:
                    split_hi(x + 1, 0)
                    spread_ids(x + 1)
                    split_hi(x + 1, 1)
                for g in early_runs(x):
                    tp_copy(0, g)
                if x == 0:
                    act.wait_ge(denT_full, 1)
                    nc.scalar.copy(den32[:, :], mlp[1][0:DENSE, :, :].rearrange("p a b -> p (a b)")
                                   ).then_inc(den32_ready, 1)
                if 3 <= x < 5:
                    act.wait_ge(parts_zero, 2)
                    act.wait_ge(den32_ready, 1)
                    q = (0, 1)[x - 3]
                    nc.scalar.copy(den_parts[32 * q:32 * q + DENSE, :], den32[:, :]).then_inc(den_hi_ready, 1)
                if 5 <= x < 7:
                    act.wait_ge(w1den_in, 16)
                    q = (0, 2)[x - 5]
                    nc.scalar.copy(w1den_parts[32 * q:32 * q + DENSE, :], w1den[:, :]).then_inc(den_hi_ready, 1)
                act.wait_ge(onehot_used, RP * (x + 1))
                nc.scalar.copy(embT[:, :, selected[x]], sel_ps[x % 2]).then_inc(sel_out, 1)
            for g in range(S - 1, NR):
                tp_copy(0, g)
            def take_layer2(group, part):
                obs, hbs = L2_PARTS[part]
                b0, b1 = GROUPS[group]
                for ob in obs if H1B - 1 in hbs else ():
                    act.wait_ge(l2_full, H2B * group + ob + 1)
                    nc.scalar.activation(h2[:, ob, b0:b1], L2_BANKS[ob][:, 0:b1 - b0], ACT.Relu,
                                         bias=b2s[:, ob:ob + 1]).then_inc(l2_out, 1)

            for kind, t, part in STEPS:
                if kind == "layer2":
                    if (t, part) == (EARLY, 0):
                        act.wait_ge(w_in, 64)
                    take_layer2(t, part)
                if kind == "gram":
                    act.wait_ge(gram_merged, t * GROUNDS + part + 1)
                    gram_copy(act, nc.scalar.copy, t, part, (2, 3), gram_act_out)
                elif kind == "transposes":
                    tp_copy(t, part)

        @block.tensor
        def _(pe):
            def transposes(t, g):
                pe.wait_ge(rows_in[t][g], 16 * len(runs[g]))
                k = t * NR + g
                if k >= 2:
                    pe.wait_ge(tp_out, k - 1)
                for i, f in enumerate(runs[g]):
                    last = nc.tensor.transpose(tp[g % 2][:, i, :], emb[:, t, gathered.index(f), :], ident[:, :])
                last.then_inc(tp_full, 1)

            def broadcast_ids(x):
                if x >= 2:
                    pe.wait_ge(idb_ready, x - 1)
                if x == 1:
                    pe.wait_ge(idT_ready, 1)
                f = selected[x]
                nc.tensor.matmul(idb_ps[x % 2], identr[:, f:f + 1].broadcast_to([P, P]), idT[:, :],
                                 start=True, stop=True).then_inc(idb_full, 1)

            def warm_up(n):
                nc.tensor.matmul(tp[0][:, 0:n, :], ident[:, :], ident[:, :].unsqueeze(1).broadcast_to([P, n, P]),
                                 start=True, stop=True)

            pe.wait_ge(ident_ready, 1)
            warm_up(4)
            pe.wait_ge(identr_ready, 1)
            pe.wait_ge(idf_ready, 2)
            for t in range(TILES):
                last = nc.tensor.matmul(idb_ps[0][:, t * P:(t + 1) * P],
                                        idr[:, t, selected[0]:selected[0] + 1].broadcast_to([P, P]), identr[:, :],
                                        start=True, stop=True)
            last.then_inc(idb_full, 1)
            for t in range(TILES):
                last = nc.tensor.transpose(mlp[0][0:NF, t, :], idf[:, t, :], ident[:, :])
            last.then_inc(idT_full, 1)
            warm_up(2)
            for x in range(S):
                if x >= 2:
                    pe.wait_ge(sel_out, x - 1)
                for c in range(RP):
                    k = x * RP + c
                    if c == 1 and x + 1 < S:
                        broadcast_ids(x + 1)
                    if c % RH == 0:
                        pe.wait_ge(hi_ready, 2 * x + c // RH + 1)
                        pe.wait_ge(lo_ready, 2 * x + c // RH + 1)
                    pe.wait_ge(onehot_ready, k + 1)
                    nc.tensor.matmul(sel_ps[x % 2], hi[0:TPART, x % 2, c, :], onehot[0:TPART, k % OH, :],
                                     start=(c == 0), stop=False)
                    nc.tensor.matmul(sel_ps[x % 2], lo[0:TPART, x % 2, c, :], onehot[0:TPART, k % OH, :],
                                     start=False, stop=(c == RP - 1)).then_inc(onehot_used, 1)
                if x == 0:
                    pe.wait_ge(den_in, 16)
                    for t in range(TILES):
                        last = nc.tensor.transpose(mlp[1][0:DENSE, t, :], den[:, t, :], ident[:, :])
                    last.then_inc(denT_full, 1)
                for g in early_runs(x):
                    transposes(0, g)
            for g in range(S - 1, NR):
                transposes(0, g)

            def gram_round(t, r):
                n = t * GROUNDS + r
                if r == 0:
                    pe.wait_ge(tp_out, (t + 1) * NR)
                if n == 0:
                    pe.wait_ge(sel_out, S)
                if n >= 2:
                    pe.wait_ge(gram_dve_out, n - 1)
                    pe.wait_ge(gram_act_out, n - 1)
                if t == TILES - 1:
                    pe.wait_ge(l1_out, H1B)
                for i in range(GQ):
                    b = t * P + QUADRANTS * (GQ * r + i)
                    quad = embT[:, b:b + QUADRANTS, :].rearrange("p s f -> p (s f)")
                    last = nc.tensor.matmul(gram[n % 2][:, i, :], quad, quad, start=True, stop=True)
                last.then_inc(gram_full, 1)

            def layer1(t, hb):
                if t == 0 and hb == 0:
                    pe.wait_ge(w1_in, 16 * len(pieces))
                    pe.wait_ge(den_lo_ready, 4)
                    pe.wait_ge(den32_ready, 1)
                pe.wait_ge(gram_dve_out, (t + 1) * GROUNDS)
                pe.wait_ge(gram_act_out, (t + 1) * GROUNDS)
                group = t // (TILES - 1)
                if group == EARLY and hb >= 2:
                    pe.wait_ge(gram_dve_out, 3 * GROUNDS - 1)
                    pe.wait_ge(gram_act_out, 3 * GROUNDS - 1)
                if group == LATE and hb == 3:
                    pe.wait_ge(l3_out, 1)
                b0, b1 = t * P, (t + 1) * P
                start, end = GROUPS[group]
                out, cols = L1_BANKS[group][hb][:, b0 - start:b1 - start], slice(hb * P, (hb + 1) * P)
                nc.tensor.matmul(out, w1den_parts[:, cols], den_parts[:, b0:b1], start=True, stop=False)
                for c in range(SLOTS):
                    last = nc.tensor.matmul(out, w1s[:, c, cols], zT[:, c, b0:b1], start=False, stop=(c == SLOTS - 1))
                if b1 == end:
                    last.then_inc(l1_full, 1)

            def layer2(group, part):
                if group == EARLY and part == 0:
                    pe.wait_ge(w_in, 64)
                obs, hbs = L2_PARTS[part]
                b0, b1 = GROUPS[group]
                for ob in obs:
                    if part == 0 and group == LATE:
                        pe.wait_ge(l2_out, ob + 1)
                    for hb in hbs:
                        pe.wait_ge(l1_out, H1B * group + max(hb, ob) + 1)
                        last = nc.tensor.matmul(L2_BANKS[ob][:, 0:b1 - b0], w2s[:, hb, ob * P:(ob + 1) * P],
                                                h1[:, hb, b0:b1], start=(hb == 0), stop=(hb == H1B - 1))
                    if H1B - 1 in hbs:
                        last.then_inc(l2_full, 1)

            def layer3(group, _):
                b0, b1 = GROUPS[group]
                if group == LATE:
                    pe.wait_ge(gram_dve_out, TILES * GROUNDS)
                    pe.wait_ge(gram_act_out, TILES * GROUNDS)
                for ob in range(H2B):
                    pe.wait_ge(l2_out, H2B * group + ob + 1)
                    last = nc.tensor.matmul(L3_BANK[group][0:1, 0:b1 - b0], w3s[:, ob:ob + 1], h2[:, ob, b0:b1],
                                            start=(ob == 0), stop=(ob == H2B - 1))
                last.then_inc(l3_full, 1)

            do = {"transposes": transposes, "gram": gram_round, "layer1": layer1, "layer2": layer2, "layer3": layer3}
            for kind, t, part in STEPS:
                do[kind](t, part)


_INS = (['dense_ctx', 'ids'] + [f'tbl_{f}' for f in range(32)]
        + ['W_top1', 'b_top1', 'W_top2', 'b_top2', 'W_top3'])


def kernel(**inputs):
    import numpy as _np
    import concourse.bacc as _bacc
    from concourse import mybir as _mybir
    from concourse.bass_utils import run_bass_kernel_spmd as _run

    nc = _bacc.Bacc("TRN2", target_bir_lowering=False, num_devices=1)
    arrays, args = {}, {}
    for name in _INS:
        a = _np.ascontiguousarray(inputs[name])
        arrays[f"in_{name}"] = a
        args[name] = nc.dram_tensor(f"in_{name}", a.shape, _mybir.dt.from_np(a.dtype), kind="ExternalInput").ap()
    y = nc.dram_tensor("out_y", (BATCH, 1), _mybir.dt.float32, kind="ExternalOutput").ap()
    dlrm_tower(nc, args['dense_ctx'], args['ids'], [args[f'tbl_{f}'] for f in range(32)],
               args['W_top1'], args['b_top1'], args['W_top2'], args['b_top2'], args['W_top3'], y)
    r = _run(nc, [arrays], core_ids=[0])
    return r.results[0]["out_y"]
```
